# Optimizing a Trainium2 kernel written in Bass

```python
import numpy as np
import jax
import jax.numpy as jnp

def _softmax(x, axis=-1):
    return jax.nn.softmax(x, axis=axis)

def _gelu(x):
    return jax.nn.gelu(x, approximate=True)

def _silu(x):
    return jax.nn.silu(x)

def _sigmoid(x):
    return jax.nn.sigmoid(x)

def _layernorm(x, axis=-1, eps=1e-05):
    m = jnp.mean(x, axis=axis, keepdims=True)
    v = jnp.var(x, axis=axis, keepdims=True)
    return (x - m) / jnp.sqrt(v + eps)

def _scatter_add(tgt, idx, src, axis=0):
    return tgt.at[idx].add(src)

def _segment_sum(src, seg, n):
    return jax.ops.segment_sum(src, seg, n)
kernel_name = 'mk_vit_tower_d2_tok_img768_r4_2e4bf3'

def setup_inputs(seed: int=0):
    np.random.seed(seed)
    _w = jnp.asarray

    def _rec_inputs():
        import jax
        import jax.numpy as jnp
        _rk = jax.random.key(seed)
        x = -0.00016672 + 0.999947 * jax.random.normal(jax.random.fold_in(_rk, 1), (16, 3, 96, 96), jnp.float32)
        return x
    x = _rec_inputs()

    def _L0_tok_setup():
        import jax, jax.numpy as jnp
        import numpy as np
        B, C, H, W = (64, 3, 96, 96)
        P = 16
        NH, NW = (H // P, W // P)
        N = NH * NW
        PATCH_DIM = C * P * P
        DIM = 192

        def _layernorm(x, g, b, eps=1e-05):
            mu = jnp.mean(x, axis=-1, keepdims=True)
            var = jnp.var(x, axis=-1, keepdims=True)
            return (x - mu) * jax.lax.rsqrt(var + eps) * g + b
        key = jax.random.key(seed)
        ks = jax.random.split(key, 8)
        img = jax.random.normal(ks[0], (B, C, H, W), dtype=jnp.float32)
        ln1_g = jnp.ones((PATCH_DIM,), jnp.float32)
        ln1_b = jnp.zeros((PATCH_DIM,), jnp.float32)
        W_lin = jax.random.normal(ks[1], (PATCH_DIM, DIM), jnp.float32) / np.sqrt(PATCH_DIM)
        b_lin = jnp.zeros((DIM,), jnp.float32)
        ln2_g = jnp.ones((DIM,), jnp.float32)
        ln2_b = jnp.zeros((DIM,), jnp.float32)
        pos_embedding = jax.random.normal(ks[2], (1, N + 1, DIM), jnp.float32)
        cls_token = jax.random.normal(ks[3], (1, 1, DIM), jnp.float32)
        return {'img': img, 'ln1_g': ln1_g, 'ln1_b': ln1_b, 'W_lin': W_lin, 'b_lin': b_lin, 'ln2_g': ln2_g, 'ln2_b': ln2_b, 'pos_embedding': pos_embedding, 'cls_token': cls_token}
    _L0_tok_all = _L0_tok_setup()
    _L0_tok_in = {k: v for k, v in _L0_tok_all.items() if k in ('ln1_g', 'ln1_b', 'W_lin', 'b_lin', 'ln2_g', 'ln2_b', 'pos_embedding', 'cls_token')}
    del _L0_tok_all

    def _L0_attn_setup():
        import jax, jax.numpy as jnp
        import numpy as np
        D_MODEL = 192
        STATE = 64
        EXPAND = 2
        D_INNER = D_MODEL * EXPAND
        BATCH = 2
        SEQ = 256

        def _selective_scan(xp, dt, A, Bm, Cm):
            b, L, d = xp.shape
            n = A.shape[0]

            def step(h, inp):
                x_t, dt_t, B_t, C_t = inp
                dA = jnp.exp(dt_t[..., None] * A)
                h = dA * h + (dt_t * x_t)[..., None] * B_t[:, None, :]
                y_t = jnp.einsum('bdn,bn->bd', h, C_t)
                return (h, y_t)
            h0 = jnp.zeros((b, d, n), xp.dtype)
            xs = (jnp.swapaxes(xp, 0, 1), jnp.swapaxes(dt, 0, 1), jnp.swapaxes(Bm, 0, 1), jnp.swapaxes(Cm, 0, 1))
            _, ys = jax.lax.scan(step, h0, xs)
            return jnp.swapaxes(ys, 0, 1)
        key = jax.random.key(seed)
        ks = jax.random.split(key, 5)

        def lin(k, fan_in, fan_out):
            bound = 1.0 / np.sqrt(fan_in)
            return jax.random.uniform(k, (fan_in, fan_out), jnp.float32, -bound, bound)
        return {'x': jax.random.normal(ks[0], (BATCH, SEQ, D_MODEL), jnp.float32), 'W_in': lin(ks[1], D_MODEL, 2 * D_INNER), 'W_x': lin(ks[2], D_INNER, 2 * STATE), 'W_dt': lin(ks[3], D_INNER, D_INNER), 'b_dt': jnp.zeros((D_INNER,), jnp.float32), 'A_log': jnp.log(jnp.arange(1, STATE + 1, dtype=jnp.float32)), 'D': jnp.ones((D_INNER,), jnp.float32), 'W_out': lin(ks[4], D_INNER, D_MODEL)}
    _L0_attn_all = _L0_attn_setup()
    _L0_attn_in = {k: v for k, v in _L0_attn_all.items() if k in ('W_in', 'W_x', 'W_dt', 'b_dt', 'A_log', 'D', 'W_out')}
    del _L0_attn_all

    def _L0_ffn_setup():
        import jax, jax.numpy as jnp
        import numpy as np
        B, SEQ, D = (2, 256, 192)
        E, H = (8, 768)
        CAPACITY = 2
        key = jax.random.key(seed)
        ks = jax.random.split(key, 6)
        x = jax.random.normal(ks[0], (B, SEQ, D), dtype=jnp.float32)
        gate_weight = jax.random.normal(ks[1], (E, D), dtype=jnp.float32) * 0.006
        w1 = jax.random.normal(ks[2], (E, D, H), dtype=jnp.float32) * (1.0 / np.sqrt(D))
        b1 = jnp.zeros((E, H), dtype=jnp.float32)
        w2 = jax.random.normal(ks[3], (E, H, D), dtype=jnp.float32) * (1.0 / np.sqrt(H))
        b2 = jnp.zeros((E, D), dtype=jnp.float32)
        return {'x': x, 'gate_weight': gate_weight, 'w1': w1, 'b1': b1, 'w2': w2, 'b2': b2}
    _L0_ffn_all = _L0_ffn_setup()
    _L0_ffn_in = {k: v for k, v in _L0_ffn_all.items() if k in ('gate_weight', 'w1', 'b1', 'w2', 'b2')}
    del _L0_ffn_all

    def _L1_attn_setup():
        import jax, jax.numpy as jnp
        import numpy as np
        EMBED = 192
        HEADS = 12
        HEAD_DIM = EMBED // HEADS
        LN_EPS = 1e-05
        key = jax.random.key(seed)
        k1, k2, k3 = jax.random.split(key, 3)
        B, T = (2, 1024)
        x = jax.random.normal(k1, (B, T, EMBED), dtype=jnp.float32)
        w_qkv = jax.random.normal(k2, (EMBED, 3 * EMBED), dtype=jnp.float32) * EMBED ** (-0.5)
        w_out = jax.random.normal(k3, (EMBED, EMBED), dtype=jnp.float32) * EMBED ** (-0.5)
        b_out = jnp.zeros((EMBED,), dtype=jnp.float32)
        ln_g = jnp.ones((EMBED,), dtype=jnp.float32)
        ln_b = jnp.zeros((EMBED,), dtype=jnp.float32)
        return {'x': x, 'w_qkv': w_qkv, 'w_out': w_out, 'b_out': b_out, 'ln_g': ln_g, 'ln_b': ln_b}
    _L1_attn_all = _L1_attn_setup()
    _L1_attn_in = {k: v for k, v in _L1_attn_all.items() if k in ('w_qkv', 'w_out', 'b_out', 'ln_g', 'ln_b')}
    del _L1_attn_all

    def _L1_ffn_setup():
        import jax, jax.numpy as jnp
        import numpy as np
        B, S, D, H, E, K = (1, 512, 192, 384, 8, 2)
        key = jax.random.key(seed)
        ks = jax.random.split(key, 6)
        scale_d = 1.0 / np.sqrt(D)
        scale_h = 1.0 / np.sqrt(H)
        return {'x': jax.random.normal(ks[0], (B, S, D), dtype=jnp.float32), 'Wg': jax.random.uniform(ks[1], (D, E), minval=-scale_d, maxval=scale_d, dtype=jnp.float32), 'W1': jax.random.uniform(ks[2], (E, D, H), minval=-scale_d, maxval=scale_d, dtype=jnp.float32), 'b1': jax.random.uniform(ks[3], (E, H), minval=-scale_d, maxval=scale_d, dtype=jnp.float32), 'W2': jax.random.uniform(ks[4], (E, H, D), minval=-scale_h, maxval=scale_h, dtype=jnp.float32), 'b2': jax.random.uniform(ks[5], (E, D), minval=-scale_h, maxval=scale_h, dtype=jnp.float32)}
    _L1_ffn_all = _L1_ffn_setup()
    _L1_ffn_in = {k: v for k, v in _L1_ffn_all.items() if k in ('Wg', 'W1', 'b1', 'W2', 'b2')}
    del _L1_ffn_all
    return {'x': x, 'L0_tok_ln1_g': _L0_tok_in['ln1_g'], 'L0_tok_ln1_b': _L0_tok_in['ln1_b'], 'L0_tok_W_lin': _L0_tok_in['W_lin'], 'L0_tok_b_lin': _L0_tok_in['b_lin'], 'L0_tok_ln2_g': _L0_tok_in['ln2_g'], 'L0_tok_ln2_b': _L0_tok_in['ln2_b'], 'L0_tok_pos_embedding': _L0_tok_in['pos_embedding'], 'L0_tok_cls_token': _L0_tok_in['cls_token'], 'L0_attn_W_in': _L0_attn_in['W_in'], 'L0_attn_W_x': _L0_attn_in['W_x'], 'L0_attn_W_dt': _L0_attn_in['W_dt'], 'L0_attn_b_dt': _L0_attn_in['b_dt'], 'L0_attn_A_log': _L0_attn_in['A_log'], 'L0_attn_D': _L0_attn_in['D'], 'L0_attn_W_out': _L0_attn_in['W_out'], 'L0_ffn_gate_weight': _L0_ffn_in['gate_weight'], 'L0_ffn_w1': _L0_ffn_in['w1'], 'L0_ffn_b1': _L0_ffn_in['b1'], 'L0_ffn_w2': _L0_ffn_in['w2'], 'L0_ffn_b2': _L0_ffn_in['b2'], 'L1_attn_w_qkv': _L1_attn_in['w_qkv'], 'L1_attn_w_out': _L1_attn_in['w_out'], 'L1_attn_b_out': _L1_attn_in['b_out'], 'L1_attn_ln_g': _L1_attn_in['ln_g'], 'L1_attn_ln_b': _L1_attn_in['ln_b'], 'L1_ffn_Wg': _L1_ffn_in['Wg'], 'L1_ffn_W1': _L1_ffn_in['W1'], 'L1_ffn_b1': _L1_ffn_in['b1'], 'L1_ffn_W2': _L1_ffn_in['W2'], 'L1_ffn_b2': _L1_ffn_in['b2']}

def reference(x, L0_tok_ln1_g, L0_tok_ln1_b, L0_tok_W_lin, L0_tok_b_lin, L0_tok_ln2_g, L0_tok_ln2_b, L0_tok_pos_embedding, L0_tok_cls_token, L0_attn_W_in, L0_attn_W_x, L0_attn_W_dt, L0_attn_b_dt, L0_attn_A_log, L0_attn_D, L0_attn_W_out, L0_ffn_gate_weight, L0_ffn_w1, L0_ffn_b1, L0_ffn_w2, L0_ffn_b2, L1_attn_w_qkv, L1_attn_w_out, L1_attn_b_out, L1_attn_ln_g, L1_attn_ln_b, L1_ffn_Wg, L1_ffn_W1, L1_ffn_b1, L1_ffn_W2, L1_ffn_b2):
    import jax
    import jax.numpy as jnp

    def _L0_tok_ref(img, ln1_g, ln1_b, W_lin, b_lin, ln2_g, ln2_b, pos_embedding, cls_token):
        import jax, jax.numpy as jnp
        import numpy as np
        B, C, H, W = (64, 3, 96, 96)
        P = 16
        NH, NW = (H // P, W // P)
        N = NH * NW
        PATCH_DIM = C * P * P
        DIM = 192

        def _layernorm(x, g, b, eps=1e-05):
            mu = jnp.mean(x, axis=-1, keepdims=True)
            var = jnp.var(x, axis=-1, keepdims=True)
            return (x - mu) * jax.lax.rsqrt(var + eps) * g + b
        b = img.shape[0]
        x = img.reshape(b, C, NH, P, NW, P)
        x = jnp.transpose(x, (0, 2, 4, 3, 5, 1))
        x = x.reshape(b, N, PATCH_DIM)
        x = _layernorm(x, ln1_g, ln1_b)
        x = jnp.einsum('bnp,pd->bnd', x, W_lin) + b_lin
        x = _layernorm(x, ln2_g, ln2_b)
        cls = jnp.broadcast_to(cls_token, (b, 1, DIM))
        x = jnp.concatenate([cls, x], axis=1)
        x = x + pos_embedding[:, :N + 1]
        return x

    def _L0_attn_ref(x, W_in, W_x, W_dt, b_dt, A_log, D, W_out):
        import jax, jax.numpy as jnp
        import numpy as np
        D_MODEL = 192
        STATE = 64
        EXPAND = 2
        D_INNER = D_MODEL * EXPAND
        BATCH = 2
        SEQ = 256

        def _selective_scan(xp, dt, A, Bm, Cm):
            b, L, d = xp.shape
            n = A.shape[0]

            def step(h, inp):
                x_t, dt_t, B_t, C_t = inp
                dA = jnp.exp(dt_t[..., None] * A)
                h = dA * h + (dt_t * x_t)[..., None] * B_t[:, None, :]
                y_t = jnp.einsum('bdn,bn->bd', h, C_t)
                return (h, y_t)
            h0 = jnp.zeros((b, d, n), xp.dtype)
            xs = (jnp.swapaxes(xp, 0, 1), jnp.swapaxes(dt, 0, 1), jnp.swapaxes(Bm, 0, 1), jnp.swapaxes(Cm, 0, 1))
            _, ys = jax.lax.scan(step, h0, xs)
            return jnp.swapaxes(ys, 0, 1)
        xz = x @ W_in
        xp, z = jnp.split(xz, 2, axis=-1)
        Bm, Cm = jnp.split(xp @ W_x, 2, axis=-1)
        dt = jax.nn.softplus(xp @ W_dt + b_dt)
        A = -jnp.exp(A_log)
        y = _selective_scan(xp, dt, A, Bm, Cm) + xp * D
        y = y * jax.nn.silu(z)
        return y @ W_out

    def _L0_ffn_ref(x, gate_weight, w1, b1, w2, b2):
        import jax, jax.numpy as jnp
        import numpy as np
        B, SEQ, D = (2, 256, 192)
        E, H = (8, 768)
        CAPACITY = 2
        Bb, s, d = x.shape
        xf = x.reshape(-1, d)
        S = xf.shape[0]
        k = S * CAPACITY
        logits = xf @ gate_weight.T
        scores = jax.nn.softmax(logits, axis=-1).T
        vals, idx = jax.lax.top_k(scores.reshape(-1), k)
        gate = jnp.zeros((E * S,), dtype=x.dtype).at[idx].add(vals).reshape(E, S)
        h = jax.nn.gelu(jnp.einsum('sd,edh->esh', xf, w1) + b1[:, None, :], approximate=True)
        out = jnp.einsum('esh,ehd->esd', h, w2) + b2[:, None, :]
        y = jnp.einsum('es,esd->sd', gate, out)
        return y.reshape(Bb, s, d)

    def _L1_attn_ref(x, w_qkv, w_out, b_out, ln_g, ln_b):
        import jax, jax.numpy as jnp
        import numpy as np
        EMBED = 192
        HEADS = 12
        HEAD_DIM = EMBED // HEADS
        LN_EPS = 1e-05
        B, T, E = x.shape
        qkv = jnp.einsum('bte,ef->btf', x, w_qkv)
        q, k, v = jnp.split(qkv, 3, axis=-1)

        def split_heads(t):
            return t.reshape(B, T, HEADS, HEAD_DIM).transpose(0, 2, 1, 3)
        q, k, v = map(split_heads, (q, k, v))
        scores = jnp.einsum('bhtd,bhsd->bhts', q, k) / jnp.sqrt(jnp.float32(HEAD_DIM))
        attn = jax.nn.softmax(scores, axis=-1)
        out = jnp.einsum('bhts,bhsd->bhtd', attn, v)
        out = out.transpose(0, 2, 1, 3).reshape(B, T, E)
        y = jnp.einsum('bte,ef->btf', out, w_out) + b_out
        mu = jnp.mean(y, axis=-1, keepdims=True)
        var = jnp.var(y, axis=-1, keepdims=True)
        y = (y - mu) * jax.lax.rsqrt(var + LN_EPS) * ln_g + ln_b
        return y

    def _L1_ffn_ref(x, Wg, W1, b1, W2, b2):
        import jax, jax.numpy as jnp
        import numpy as np
        B, S, D, H, E, K = (1, 512, 192, 384, 8, 2)
        gate_scores = jnp.einsum('bsd,de->bse', x, Wg)
        topk_scores, topk_idx = jax.lax.top_k(gate_scores, K)
        topk_probs = jax.nn.softmax(topk_scores, axis=-1)
        h = jax.nn.gelu(jnp.einsum('bsd,edh->bseh', x, W1) + b1, approximate=False)
        y = jnp.einsum('bseh,eho->bseo', h, W2) + b2
        y_sel = jnp.take_along_axis(y, topk_idx[..., None], axis=2)
        return jnp.sum(topk_probs[..., None] * y_sel, axis=2)
    h = _L0_tok_ref(x, L0_tok_ln1_g, L0_tok_ln1_b, L0_tok_W_lin, L0_tok_b_lin, L0_tok_ln2_g, L0_tok_ln2_b, L0_tok_pos_embedding, L0_tok_cls_token)
    h = h + _L0_attn_ref(_layernorm(h, axis=-1), L0_attn_W_in, L0_attn_W_x, L0_attn_W_dt, L0_attn_b_dt, L0_attn_A_log, L0_attn_D, L0_attn_W_out)
    h = h + _L0_ffn_ref(_layernorm(h, axis=-1), L0_ffn_gate_weight, L0_ffn_w1, L0_ffn_b1, L0_ffn_w2, L0_ffn_b2)
    h = h + _L1_attn_ref(_layernorm(h, axis=-1), L1_attn_w_qkv, L1_attn_w_out, L1_attn_b_out, L1_attn_ln_g, L1_attn_ln_b)
    h = h + _L1_ffn_ref(_layernorm(h, axis=-1), L1_ffn_Wg, L1_ffn_W1, L1_ffn_b1, L1_ffn_W2, L1_ffn_b2)
    return h

_drawn_inputs = setup_inputs


def setup_inputs(seed=0):
    import zlib

    import numpy as np

    out = dict(_drawn_inputs(seed))
    spreads = {'L0_tok_ln1_g': (1.0, 0.2),
     'L0_tok_ln1_b': (0.0, 0.1),
     'L0_tok_b_lin': (0.0, 0.1),
     'L0_tok_ln2_g': (1.0, 0.2),
     'L0_tok_ln2_b': (0.0, 0.1),
     'L0_attn_b_dt': (0.0, 0.8),
     'L0_attn_D': (1.0, 0.6),
     'L0_ffn_b1': (0.0, 0.491),
     'L0_ffn_b2': (0.0, 0.37),
     'L1_attn_b_out': (0.0, 0.1),
     'L1_attn_ln_g': (1.0, 0.2),
     'L1_attn_ln_b': (0.0, 0.1)}
    factors = {'L0_attn_W_dt': 3.367, 'L0_attn_A_log': 7.464, 'L1_ffn_b1': 8.0, 'L1_ffn_b2': 4.734}
    for name, (base, spread) in spreads.items():
        noise = np.random.default_rng([zlib.crc32(name.encode()), seed]).standard_normal(out[name].shape)
        drawn = base * np.exp(spread * noise) if base else spread * noise
        out[name] = jnp.asarray(drawn.astype(out[name].dtype))
    for name, factor in factors.items():
        out[name] = (out[name] * factor).astype(out[name].dtype)
    return out
```

```python
from contextlib import ExitStack

import concourse.bass as bass
from concourse import mybir

ALU = mybir.AluOpType
ACT = mybir.ActivationFunctionType
F32 = mybir.dt.float32
BF16 = mybir.dt.bfloat16
I32 = mybir.dt.int32
AX_X = mybir.AxisListType.X

B, CH, IMG, PATCH = 16, 3, 96, 16
G = IMG // PATCH
N = G * G
T = N + 1
TOK = B * T
D = 192
P = 96
K = D // P
PD = CH * PATCH * PATCH
DI = 2 * D
KI = DI // P
NS = 64
E = 8
NH, HD = 12, 16
HG = 4
NG = NH // HG
EPS = 1e-5
BANK = 512
TT5 = 5
TPAD = TT5 * 128
HALVES = ((0, TOK // 2), (TOK // 2, TOK))
WIDE = ((0, BANK), (BANK, TOK))

ROW_BLIN, ROW_LN2G, ROW_LN2B, ROW_BDT, ROW_D = 0, 2, 4, 6, 10
ROW_BOUT, ROW_LNG, ROW_LNB, ROW_GW, ROW_CLS, ROW_POS = 14, 16, 18, 20, 36, 38
NROWS = ROW_POS + 2 * T
H0, H1 = 768, 384
ROW_B0, ROW_B1 = 0, E * H0 // 128
NROWS_B = ROW_B1 + E * H1 // 128


def layer_norm_sems(sem):
    return {n: sem(f"norm_{n}") for n in ("mean", "centred", "squared", "var", "std", "rstd", "out")}


LN2, LN_SCAN, LN_MOE0, LN_ATT, LN_OUT, LN_MOE1 = (2 * n for n in range(6))


def layer_norm_pe(pe, s, x, sq, over, mean_ps, var_ps, pieces):
    for p, (a, b) in enumerate(pieces):
        for k in range(K):
            mm = pe.matmul(mean_ps[p][0:P, 0:b - a], over, x[:, k, a:b], start=(k == 0), stop=(k == K - 1))
        mm.then_inc(s["mean"], 1)
    for p, (a, b) in enumerate(pieces):
        pe.wait_ge(s["squared"], s["base"] + p + 1)
        for k in range(K):
            mm = pe.matmul(var_ps[p][0:P, 0:b - a], over, sq[:, k, a:b], start=(k == 0), stop=(k == K - 1))
        mm.then_inc(s["var"], 1)


def layer_norm_act(act, s, xc, sq, std, eps, var_ps, pieces):
    for p, (a, b) in enumerate(pieces):
        act.wait_ge(s["centred"], s["base"] + p + 1)
        act.activation(sq[:, :, a:b], xc[:, :, a:b], ACT.Square).then_inc(s["squared"], 1)
    for p, (a, b) in enumerate(pieces):
        act.wait_ge(s["var"], s["base"] + p + 1)
        act.activation(std[:, a:b], var_ps[p][0:P, 0:b - a], ACT.Sqrt, bias=eps).then_inc(s["std"], 1)


def layer_norm_dve(dve, s, x, xc, std, out, mean_ps, pieces):
    for p, (a, b) in enumerate(pieces):
        dve.wait_ge(s["mean"], s["base"] + p + 1)
        dve.tensor_tensor(xc[:, :, a:b], x[:, :, a:b],
                          mean_ps[p][0:P, 0:b - a].unsqueeze(1).to_broadcast([P, K, b - a]),
                          ALU.subtract).then_inc(s["centred"], 1)
    for p, (a, b) in enumerate(pieces):
        dve.wait_ge(s["std"], s["base"] + p + 1)
        dve.reciprocal(std[:, a:b], std[:, a:b]).then_inc(s["rstd"], 1)
        dve.wait_ge(s["rstd"], s["base"] + p + 1)
        dve.tensor_tensor(out[:, :, a:b], xc[:, :, a:b],
                          std[:, a:b].unsqueeze(1).to_broadcast([P, K, b - a]),
                          ALU.mult).then_inc(s["out"], 1)


def build_tower(nc, A, out):
    with ExitStack() as whole:
        def sem(name):
            return whole.enter_context(nc.semaphore(name))

        def sb_in(ctx, tag=""):
            return lambda name, shape, dt=F32: ctx.enter_context(nc.sbuf_tensor(tag + name, shape, dt))

        sb = sb_in(whole)
        PS = whole.enter_context(nc.psum_tensor("PS", [128, 8 * BANK], F32))

        def bank(i, n=1):
            return PS[:, i * BANK:(i + n) * BANK]

        h = sb("h", [P, K, TOK])
        ident = sb("ident", [128, 128])
        over = sb("over", [P, P])
        ones = sb("ones", [128, 128])
        eps = sb("eps", [128, 1])
        V = sb("V", [P, NROWS])
        VB = sb("VB", [128, NROWS_B])
        xn = sb("xn", [P, K, TPAD])
        xc = sb("xc", [P, K, TOK])
        sq = sb("sq", [P, K, TOK])
        std = sb("std", [P, TOK])
        norm = layer_norm_sems(sem)

        build_tokens(nc, A, sem, sb_in, bank, locals())
        build_scan_block(nc, A, sem, sb_in, bank, locals())
        build_moe(nc, A, sem, sb_in, bank, locals(), layer=0)
        build_attention(nc, A, sem, sb_in, bank, locals())
        build_moe(nc, A, sem, sb_in, bank, locals(), layer=1, out=out)


def build_tokens(nc, A, sem, sb_in, bank, g):
    h, ident, over, ones, eps, V, VB = (g[n] for n in ("h", "ident", "over", "ones", "eps", "V", "VB"))
    xc, sq, std = (g[n] for n in ("xc", "sq", "std"))
    NP = B * N
    pieces = ((0, NP // 2), (NP // 2, NP))
    with ExitStack() as ctx:
        sb = sb_in(ctx)
        img = sb("img", [B * G, CH, PATCH, G, PATCH])
        normed = sb("normed", [B * G, G, CH * PATCH, PATCH])
        rows = sb("rows", [NROWS, P])
        rows_b = sb("rows_b", [NROWS_B, 128])
        rows_1 = sb("rows_1", [4, PD // 2])
        col_1 = sb("col_1", [128, CH, 4])
        wl = sb("wl", [128, CH, 2, D])
        stats = sb("stats", [B * G, G, 2, 6])
        mv = sb("mv", [B * G, G, 2])
        rstd1 = sb("rstd1", [B * G, G])
        xT = sb("xT", [128, 2 * CH, NP])
        y0 = sb("y0", [P, K, NP])
        y1 = sb("y1", [P, K, NP])
        cp = sb("cp", [P, K])

        s_img = sem("img_loaded")
        s_rows = sem("rows_loaded")
        s_rows1 = sem("rows1_loaded")
        s_wl = sem("wl_loaded")
        s_const = sem("const_set")
        s_ident = sem("ident_set")
        s_stat = sem("patch_stats")
        s_aggr = sem("patch_aggr")
        s_pstd = sem("patch_std")
        s_prstd = sem("patch_rstd")
        s_norm = sem("patch_normed")
        s_vecT = sem("vectors_transposed")
        s_vec = sem("vectors_copied")
        s_pT = sem("patches_transposed")
        s_pTe = sem("patches_evacuated")
        s_lin = sem("lin_done")
        s_y0 = sem("y0_ready")
        s_aff = sem("ln2_affine")
        s_cls = sem("cls_sum")
        L = dict(g["norm"], base=LN2)

        x_v = A["x"].rearrange("b c (g p) w -> b g c (p w)", g=G)
        with nc.Block() as block:
            @block.sync
            def _(sp):
                for c in range(CH):
                    for b in range(B):
                        sp.dma_start(img[b * G:(b + 1) * G, c, :, :, :].rearrange("g p n w -> g (p n w)"),
                                     x_v[b, :, c, :]).then_inc(s_img, 16)

            @block.gpsimd
            def _(pool):
                pool.memset(ident[:, :], 0.0).then_inc(s_const, 1)
                pool.memset(ones[:, :], 1.0).then_inc(s_const, 1)
                pool.memset(over[:, :], 1.0 / D).then_inc(s_const, 1)
                pool.memset(eps[:, :], EPS).then_inc(s_const, 1)
                pool.wait_ge(s_const, 4)
                pool.affine_select(out=ident[:, :], in_=ident[:, :], compare_op=ALU.not_equal, fill=1.0,
                                   base=0, pattern=[[-1, 128]], channel_multiplier=1).then_inc(s_ident, 1)

            @block.scalar
            def _(act):
                for name, row, n in (("L0_tok_b_lin", ROW_BLIN, 2), ("L0_tok_ln2_g", ROW_LN2G, 2),
                                     ("L0_tok_ln2_b", ROW_LN2B, 2), ("L0_attn_b_dt", ROW_BDT, 4),
                                     ("L0_attn_D", ROW_D, 4), ("L1_attn_b_out", ROW_BOUT, 2),
                                     ("L1_attn_ln_g", ROW_LNG, 2), ("L1_attn_ln_b", ROW_LNB, 2)):
                    act.dma_start(rows[row:row + n, :], A[name].rearrange("(r p) -> r p", p=P)).then_inc(s_rows, 16)
                act.dma_start(rows[ROW_GW:ROW_GW + 2 * E, :],
                              A["L0_ffn_gate_weight"].rearrange("e (r p) -> (e r) p", p=P)).then_inc(s_rows, 16)
                act.dma_start(rows[ROW_CLS:ROW_CLS + 2, :],
                              A["L0_tok_cls_token"].rearrange("a b (r p) -> (a b r) p", p=P)).then_inc(s_rows, 16)
                act.dma_start(rows[ROW_POS:NROWS, :],
                              A["L0_tok_pos_embedding"].rearrange("a t (r p) -> (a t r) p", p=P)).then_inc(s_rows, 16)
                act.dma_start(rows_b[ROW_B0:ROW_B1, :],
                              A["L0_ffn_b1"].rearrange("e (r p) -> (e r) p", p=128)).then_inc(s_rows, 16)
                act.dma_start(rows_b[ROW_B1:NROWS_B, :],
                              A["L1_ffn_b1"].rearrange("e (r p) -> (e r) p", p=128)).then_inc(s_rows, 16)
                act.dma_start(rows_1[0:2, :], A["L0_tok_ln1_g"].rearrange("(r p) -> r p", r=2)).then_inc(s_rows1, 16)
                act.dma_start(rows_1[2:4, :], A["L0_tok_ln1_b"].rearrange("(r p) -> r p", r=2)).then_inc(s_rows1, 16)
                w_v = A["L0_tok_W_lin"].rearrange("(u k c) d -> k c u d", u=2, c=CH)
                for c in range(CH):
                    act.dma_start(wl[:, c, :, :], w_v[:, c, :, :]).then_inc(s_wl, 16)
                act.wait_ge(s_const, 4)
                act.wait_ge(s_aggr, G)
                act.activation(rstd1[:, :], mv[:, :, 1], ACT.Sqrt, bias=eps[0:B * G, :]).then_inc(s_pstd, 1)
                act.wait_ge(s_vec, 3)
                for j in range(2 * CH):
                    c, u = j // 2, j % 2
                    act.wait_ge(s_pT, j + 1)
                    act.activation(
                        xT[:, j, :].rearrange("p (q i n) -> p i n q", i=2, n=3),
                        bank(2 * (j % 2), 2).rearrange("p (i f) -> p i f", i=2)[:, :, 0:3 * B * G]
                        .rearrange("p i (n q) -> p i n q", n=3),
                        ACT.Identity, bias=col_1[:, c, 2 + u:3 + u], scale=col_1[:, c, u:u + 1]).then_inc(s_pTe, 1)
                for m in range(K):
                    for p, (a, b) in enumerate(pieces):
                        act.wait_ge(s_lin, 2 * m + p + 1)
                        act.activation(y0[:, m, a:b], bank(4 + 2 * m + p)[0:P, 0:b - a], ACT.Identity,
                                       bias=V[:, ROW_BLIN + m:ROW_BLIN + m + 1]).then_inc(s_y0, 1)
                layer_norm_act(act, L, xc, sq, std, eps[0:P, :], [bank(2), bank(3)], pieces)
                act.wait_ge(L["out"], L["base"] + 2)
                for k in range(K):
                    act.activation(y0[:, k, :], y1[:, k, :], ACT.Identity,
                                   bias=V[:, ROW_LN2B + k:ROW_LN2B + k + 1],
                                   scale=V[:, ROW_LN2G + k:ROW_LN2G + k + 1]).then_inc(s_aff, 1)

            @block.tensor
            def _(pe):
                pe.wait_ge(s_ident, 1)
                pe.wait_ge(s_rows, 13 * 16)
                pe.transpose(bank(7)[0:P, 0:NROWS], rows[:, :], ident[0:NROWS, 0:NROWS]).then_inc(s_vecT, 1)
                pe.transpose(bank(6)[:, 0:NROWS_B], rows_b[:, :], ident[0:NROWS_B, 0:NROWS_B]).then_inc(s_vecT, 1)
                pe.wait_ge(s_rows1, 32)
                r1 = rows_1[:, :].rearrange("r (k c) -> r c k", c=CH)
                for c in range(CH):
                    t = pe.transpose(bank(5)[:, 4 * c:4 * c + 4], r1[:, c, :], ident[0:4, 0:4])
                t.then_inc(s_vecT, 1)
                pe.wait_ge(s_norm, G)
                for j in range(2 * CH):
                    c, u = j // 2, j % 2
                    if j >= 2:
                        pe.wait_ge(s_pTe, j - 1)
                    for n in range(G):
                        col = BANK * (n // 3) + (n % 3) * B * G
                        t = pe.transpose(bank(2 * (j % 2), 2)[:, col:col + B * G],
                                         normed[:, n, 8 * j:8 * j + 8, :].rearrange("q r w -> q (r w)"), ident[0:B * G, 0:B * G])
                    t.then_inc(s_pT, 1)
                pe.wait_ge(s_pTe, 2 * CH)
                pe.wait_ge(s_wl, 16 * CH)
                pe.wait_ge(s_vec, 3)
                for m in range(K):
                    for p, (a, b) in enumerate(pieces):
                        for j in range(2 * CH):
                            mm = pe.matmul(bank(4 + 2 * m + p)[0:P, 0:b - a], wl[:, j // 2, j % 2, m * P:(m + 1) * P],
                                           xT[:, j, a:b], start=(j == 0), stop=(j == 2 * CH - 1))
                        mm.then_inc(s_lin, 1)
                pe.wait_ge(s_y0, 4)
                layer_norm_pe(pe, L, y0, sq, over[:, :], [bank(0), bank(1)], [bank(2), bank(3)], pieces)

            @block.vector
            def _(dve):
                dve.wait_ge(s_img, 16 * CH * B)
                flat = img[:, :, :, :, :].rearrange("q c p n w -> q (c p) n w")
                for n in range(G):
                    for i in range(2):
                        dve.bn_stats(stats[:, n, i, :], flat[:, 24 * i:24 * i + 24, n, :]).then_inc(s_stat, 1)
                for n in range(G):
                    dve.wait_ge(s_stat, 2 * n + 2)
                    dve.bn_aggr(mv[:, n, :], stats[:, n, :, :].rearrange("q i s -> q (i s)")).then_inc(s_aggr, 1)
                dve.wait_ge(s_pstd, 1)
                dve.reciprocal(rstd1[:, :], rstd1[:, :]).then_inc(s_prstd, 1)
                dve.wait_ge(s_prstd, 1)
                for n in range(G):
                    dve.tensor_scalar(normed[:, n, :, :], flat[:, :, n, :], mv[:, n, 0:1], rstd1[:, n:n + 1],
                                      ALU.subtract, ALU.mult).then_inc(s_norm, 1)
                dve.wait_ge(s_vecT, 3)
                dve.tensor_copy(V[:, :], bank(7)[0:P, 0:NROWS]).then_inc(s_vec, 1)
                dve.tensor_copy(VB[:, :], bank(6)[:, 0:NROWS_B]).then_inc(s_vec, 1)
                dve.tensor_copy(col_1[:, :, :].rearrange("p c r -> p (c r)"), bank(5)[:, 0:4 * CH]).then_inc(s_vec, 1)
                layer_norm_dve(dve, L, y0, xc, std, y1, [bank(0), bank(1)], pieces)
                dve.wait_ge(s_vec, 3)
                pos = V[:, ROW_POS:NROWS].rearrange("p (t k) -> p k t", k=K)
                dve.tensor_tensor(cp[:, :], V[:, ROW_CLS:ROW_CLS + K], pos[:, :, 0], ALU.add).then_inc(s_cls, 1)
                dve.wait_ge(s_cls, 1)
                for k in range(K):
                    hv = h[:, k, :].rearrange("p (b t) -> p b t", t=T)
                    dve.tensor_copy(hv[:, :, 0:1], cp[:, k:k + 1].unsqueeze(1).to_broadcast([P, B, 1]))
                    dve.wait_ge(s_aff, k + 1)
                    dve.tensor_tensor(hv[:, :, 1:T], y0[:, k, :].rearrange("p (b t) -> p b t", t=N),
                                      pos[:, k, 1:T].unsqueeze(1).to_broadcast([P, B, N]), ALU.add)


def build_scan_block(nc, A, sem, sb_in, bank, g):
    h, ident, over, ones, eps, V = (g[n] for n in ("h", "ident", "over", "ones", "eps", "V"))
    xn, xc, sq, std = (g[n] for n in ("xn", "xc", "sq", "std"))
    GRP = P // 4
    COLS = GRP * T
    STEPS = DI // 2 // GRP
    ROWS = 2 * 3 * KI
    bc_d = nc.dram_tensor("bc_rows", [B, ROWS, P, T], BF16).ap()
    with ExitStack() as ctx:
        sb = sb_in(ctx)
        sel = sb("sel", [ROWS, 2, 2, 128], BF16)
        a_neg = sb("a_neg", [128, 1])
        Bs = sb("Bs", [128, TOK])
        Cs = sb("Cs", [128, TOK])
        c_diag = sb("c_diag", [128, 2, T * (2 * T + 1) + T])
        parts = sb("parts", [P, 2, 3, KI, TOK], BF16)
        silu = sb("silu", [P, KI, TOK])
        yT = sb("yT", [P, KI, TOK])
        w_out = sb("w_out", [P, KI, D])

        s_wout = sem("wout_loaded")
        with ExitStack() as ctx2:
            sb2 = sb_in(ctx2)
            w_in = sb2("w_in", [P, K, 2 * DI])
            w_b = sb2("w_b", [P, KI, 2, NS])
            w_c = sb2("w_c", [P, KI, 2, NS])
            w_dt = sb2("w_dt", [P, KI, DI])
            xp = sb2("xp", [P, KI, TOK])
            v = sb2("v", [P, KI, TOK])
            e = sb2("e", [P, KI, TOK])
            l = sb2("l", [P, KI, TOK])
            dt = sb2("dt", [P, KI, TOK])
            dtx = l
            res = [v, e]

            s_w = sem("scan_weights")
            s_selz = sem("sel_zeroed")
            s_sel = sem("sel_set")
            s_al = sem("a_log_loaded")
            s_ae = sem("a_exp")
            s_a = sem("a_ready")
            s_cz = sem("c_zeroed")
            s_pj = sem("proj_done")
            s_evd = sem("proj_copied_dve")
            s_eva = sem("proj_copied_act")
            s_abs = sem("dt_abs")
            s_exp = sem("dt_exp")
            s_ln = sem("dt_ln")
            s_lo = sem("dt_low")
            s_cor = sem("dt_corr")
            s_sum = sem("dt_logsum")
            s_dt = sem("dt_ready")
            s_dtx = sem("dtx_ready")
            s_z0 = sem("dt_zeroed")
            s_hi = sem("part_hi")
            s_r1 = sem("part_r1")
            s_mid = sem("part_mid")
            s_low = sem("part_lo")
            L = dict(g["norm"], base=LN_SCAN)
            with nc.Block() as block:
                @block.sync
                def _(sp):
                    sp.dma_start(w_in[:, :, :], A["L0_attn_W_in"].rearrange("(k p) d -> p k d", p=P)).then_inc(s_w, 16)
                    sp.dma_start(w_dt[:, :, :], A["L0_attn_W_dt"].rearrange("(k p) d -> p k d", p=P)).then_inc(s_w, 16)
                    wx = A["L0_attn_W_x"].rearrange("(k p) d -> p k d", p=P)
                    for u in range(2):
                        sp.dma_start(w_b[:, :, u, :], wx[:, :, 0:NS]).then_inc(s_w, 16)
                        sp.dma_start(w_c[:, :, u, :], wx[:, :, NS:2 * NS]).then_inc(s_w, 16)
                        sp.dma_start(a_neg[u * NS:(u + 1) * NS, :],
                                     A["L0_attn_A_log"].rearrange("(n a) -> n a", a=1)).then_inc(s_al, 16)
                    sp.dma_start(w_out[:, :, :], A["L0_attn_W_out"].rearrange("(k p) d -> p k d", p=P)).then_inc(s_wout, 16)

                @block.gpsimd
                def _(pool):
                    pool.memset(c_diag[:, :, :], 0.0).then_inc(s_cz, 1)
                    pool.memset(sel[:, :, :, :], 0.0).then_inc(s_selz, 1)
                    pool.wait_ge(s_selz, 1)
                    n = 0
                    for part in range(3):
                        for half in range(2):
                            sv = sel[:, :, :, half * NS:(half + 1) * NS]
                            pool.affine_select(out=sv, in_=sv, compare_op=ALU.not_equal, fill=1.0,
                                               base=-(part * KI + 2 * half), pattern=[[-3 * KI, 2], [-1, 2], [0, NS]],
                                               channel_multiplier=1).then_inc(s_sel, 1)
                            n += 1
                            pool.wait_ge(s_sel, n)
                    for m in range(KI):
                        pool.wait_ge(s_lo, m + 1)
                        pool.tensor_tensor(dt[:, m, :], e[:, m, :], dt[:, m, :], ALU.subtract).then_inc(s_cor, 1)
                    for m in range(KI):
                        pool.wait_ge(s_hi, KI + m + 1)
                        pool.tensor_tensor(res[1][:, m, :], dtx[:, m, :], parts[:, 1, 0, m, :], ALU.subtract).then_inc(s_r1, 1)
                    for m in range(KI):
                        pool.wait_ge(s_mid, KI + m + 1)
                        pool.tensor_tensor(parts[:, 1, 2, m, :], res[1][:, m, :], parts[:, 1, 1, m, :], ALU.subtract)

                @block.tensor
                def _(pe):
                    layer_norm_pe(pe, L, h, sq, over[:, :], [bank(0), bank(1)], [bank(2), bank(3)], HALVES)
                    pe.wait_ge(s_w, 6 * 16)
                    pe.wait_ge(L["out"], L["base"] + 2)

                    def project(grp, lhs, rhs, kk, width):
                        if grp >= 4:
                            if grp - 4 <= 8:
                                pe.wait_ge(s_evd, grp - 3)
                            else:
                                pe.wait_ge(s_eva, grp - 12)
                        o = bank(2 * (grp % 4), 2)
                        for a, b in WIDE:
                            for k in range(kk):
                                mm = pe.matmul(o[0:width, a:b], lhs[:, k, :], rhs[:, k, a:b], start=(k == 0), stop=(k == kk - 1))
                        mm.then_inc(s_pj, 1)

                    for m in range(KI):
                        project(m, w_in[:, :, m * P:(m + 1) * P], xn, K, P)
                    pe.wait_ge(s_evd, KI)
                    for m in range(KI):
                        project(KI + m, w_dt[:, :, m * P:(m + 1) * P], xp, KI, P)
                    project(8, w_b[:, :, :, :].rearrange("p k u n -> p k (u n)"), xp, KI, 128)
                    project(9, w_c[:, :, :, :].rearrange("p k u n -> p k (u n)"), xp, KI, 128)
                    for m in range(KI):
                        project(10 + m, w_in[:, :, DI + m * P:DI + (m + 1) * P], xn, K, P)

                @block.scalar
                def _(act):
                    layer_norm_act(act, L, xc, sq, std, eps[0:P, :], [bank(2), bank(3)], HALVES)
                    act.wait_ge(s_al, 32)
                    act.activation(a_neg[:, :], a_neg[:, :], ACT.Exp).then_inc(s_ae, 1)
                    act.wait_ge(s_ae, 1)
                    act.mul(a_neg[:, :], a_neg[:, :], -1.0).then_inc(s_a, 1)
                    for m in range(KI):
                        act.wait_ge(s_evd, KI + m + 1)
                        act.activation(e[:, m, :], v[:, m, :], ACT.Abs).then_inc(s_abs, 1)
                        act.wait_ge(s_abs, m + 1)
                        act.activation(e[:, m, :], e[:, m, :], ACT.Exp, scale=-1.0).then_inc(s_exp, 1)
                        act.wait_ge(s_exp, m + 1)
                        act.activation(l[:, m, :], e[:, m, :], ACT.Ln, bias=1.0).then_inc(s_ln, 1)
                    act.wait_ge(s_cz, 1)
                    act.wait_ge(s_pj, 10)
                    act.copy(Cs[:, :], bank(2, 2)[:, 0:TOK]).then_inc(s_eva, 1)
                    for w in range(2):
                        for m in range(KI):
                            act.wait_ge(s_z0 if w == 0 else s_dtx, m + 1)
                            act.copy(parts[:, w, 0, m, :], (dt, dtx)[w][:, m, :]).then_inc(s_hi, 1)
                    for w in range(2):
                        for m in range(KI):
                            act.wait_ge(s_low if w == 0 else s_r1, m + 1)
                            act.copy(parts[:, w, 1, m, :], res[w][:, m, :]).then_inc(s_mid, 1)
                    for m in range(KI):
                        act.wait_ge(s_pj, 11 + m)
                        act.activation(silu[:, m, :], bank(2 * ((10 + m) % 4), 2)[0:P, 0:TOK], ACT.Silu).then_inc(s_eva, 1)

                @block.vector
                def _(dve):
                    layer_norm_dve(dve, L, h, xc, std, xn, [bank(0), bank(1)], HALVES)
                    for m in range(KI):
                        dve.wait_ge(s_pj, m + 1)
                        dve.tensor_copy(xp[:, m, :], bank(2 * m, 2)[0:P, 0:TOK]).then_inc(s_evd, 1)
                    for m in range(KI):
                        dve.wait_ge(s_pj, KI + m + 1)
                        dve.tensor_scalar(v[:, m, :], bank(2 * m, 2)[0:P, 0:TOK], V[:, ROW_BDT + m:ROW_BDT + m + 1], None,
                                          ALU.add).then_inc(s_evd, 1)
                    dve.wait_ge(s_pj, 9)
                    dve.tensor_copy(Bs[:, :], bank(0, 2)[:, 0:TOK]).then_inc(s_evd, 1)
                    dve.wait_ge(s_evd, KI)
                    for m in range(KI):
                        dve.tensor_scalar(yT[:, m, :], xp[:, m, :], V[:, ROW_D + m:ROW_D + m + 1], None, ALU.mult)
                    for m in range(KI):
                        dve.wait_ge(s_exp, m + 1)
                        dve.tensor_scalar(dt[:, m, :], e[:, m, :], 1.0, -1.0, ALU.add, ALU.add).then_inc(s_lo, 1)
                    for m in range(KI):
                        dve.wait_ge(s_cor, m + 1)
                        dve.wait_ge(s_ln, m + 1)
                        dve.tensor_tensor(l[:, m, :], l[:, m, :], dt[:, m, :], ALU.add).then_inc(s_sum, 1)
                        dve.wait_ge(s_sum, m + 1)
                        dve.scalar_tensor_tensor(dt[:, m, :], v[:, m, :], 0.0, l[:, m, :], ALU.max, ALU.add).then_inc(s_dt, 1)
                    for m in range(KI):
                        dve.wait_ge(s_dt, m + 1)
                        dve.tensor_tensor(dtx[:, m, :], dt[:, m, :], xp[:, m, :], ALU.mult).then_inc(s_dtx, 1)
                    for m in range(KI):
                        dve.wait_ge(s_dtx, m + 1)
                        dve.memset(dt[:, m, :].rearrange("p (b t) -> p b t", t=T)[:, :, 0:1], 0.0).then_inc(s_z0, 1)
                    for m in range(KI):
                        dve.wait_ge(s_hi, m + 1)
                        dve.tensor_tensor(res[0][:, m, :], dt[:, m, :], parts[:, 0, 0, m, :], ALU.subtract).then_inc(s_low, 1)
                    for m in range(KI):
                        dve.wait_ge(s_mid, m + 1)
                        dve.tensor_tensor(parts[:, 0, 2, m, :], res[0][:, m, :], parts[:, 0, 1, m, :], ALU.subtract)

        sb3 = sb_in(ctx)
        rows = sb3("rows_bc", [ROWS, 2, P * T], BF16)
        xs = sb3("xs", [128, 4, COLS])
        u_ = sb3("u", [128, 4, COLS])
        hs = sb3("hs", [128, 2, 2, P, T])
        y_tok = sb3("y_tok", [2 * T, 2, DI // 2])
        bb = sb3("bb", [128, 2, T])

        s_wr = [sem("rows_stored_0"), sem("rows_stored_1")]
        s_rd = [sem("rows_loaded_0"), sem("rows_loaded_1")]
        s_cb = sem("c_copied")
        s_bb = sem("b_copied")
        s_pdt = sem("dt_spread")
        s_px = sem("dtx_spread")
        s_da = sem("decay_ready")
        s_xs = sem("dtx_copied")
        s_u = sem("u_from_pool")
        s_ud = sem("u_from_dve")
        s_sc = sem("scanned")
        s_y = sem("y_summed")
        s_yc = sem("y_copied")
        s_yt = sem("y_transposed")

        PST = STEPS - 1
        LEAD = 2
        share = [T * s // STEPS for s in range(STEPS + 1)]
        Y_STEP = 1

        def decay_ps(c):
            return bank(2 * (c % 2), 2)[:, 0:COLS]

        x_ps = bank(4, 2)[:, 0:COLS]

        def wait_count(eng, s, count):
            if not (isinstance(count, int) and count <= 0):
                eng.wait_ge(s, count)

        def ahead(b, c):
            return (0, c + LEAD) if c + LEAD < STEPS else (1, c + LEAD - STEPS)

        def images(eng, image):
            for b in range(2):
                image(b, 0, b)
            with eng.Fori(1, B // 2 - 1) as i:
                for slot in range(2):
                    image(2 * i + slot, i, slot)
            for slot in range(2):
                image(B - 2 + slot, B // 2 - 1, slot, last=(slot == 1))

        with nc.Block() as block:
            @block.sync
            def _(sp):
                def store(b, slot):
                    sp.dma_start(bc_d[bass.ds(b, 1)].rearrange("a r p t -> p (a r) t"),
                                 parts[:, :, :, :, bass.ds(b * T, T)].rearrange("p w i k t -> p (w i k) t")
                                 ).then_inc(s_wr[slot], 16)

                def load(b, slot):
                    sp.dma_start(rows[:, slot, :], bc_d[bass.ds(b, 1)].rearrange("a r p t -> (a r) (p t)")
                                 ).then_inc(s_rd[slot], 16)

                store(0, 0)
                store(1, 1)
                for b in range(2):
                    sp.wait_ge(s_wr[b], 16)
                    load(b, b)
                    store(b + 2, b)
                with sp.Fori(1, B // 2 - 1) as i:
                    for slot in range(2):
                        sp.wait_ge(s_pdt, STEPS * (2 * i + slot - 1))
                        sp.wait_ge(s_wr[slot], 16 * (i + 1))
                        load(2 * i + slot, slot)
                        store(2 * i + slot + 2, slot)
                for b in range(B - 2, B):
                    sp.wait_ge(s_wr[b % 2], 16 * (b // 2 + 1))
                    sp.wait_ge(s_pdt, STEPS * (b - 1))
                    load(b, b % 2)

            @block.tensor
            def _(pe):
                def spread(out, w, c, slot, done):
                    at = (c % (STEPS // 2)) * COLS
                    for x0, x1 in ((0, BANK), (BANK, COLS)):
                        mm = pe.matmul(out[:, x0:x1], sel[:, w, c // (STEPS // 2), :],
                                       rows[:, slot, at + x0:at + x1], start=True, stop=True)
                    mm.then_inc(done, 1)

                def spread_x(b, turn, c, slot):
                    if c == 0:
                        pe.wait_ge(s_rd[slot], 16 * (turn + 1))
                        wait_count(pe, s_ud, b)
                    else:
                        wait_count(pe, s_xs, PST * b + c)
                    spread(x_ps, 1, c, slot, s_px)

                def sums(slot, first, last):
                    for t in range(first, last):
                        mm = pe.matmul(bank(6 + slot)[0:2 * T, 0:DI // 2],
                                       c_diag[:, slot, 2 * T * t:2 * T * (t + 1)], hs[:, slot, :, :, t].rearrange("p c f -> p (c f)"),
                                       start=(t == 0), stop=(t == T - 1))
                    if last == T:
                        mm.then_inc(s_y, 1)

                def turn_y(b, slot):
                    pe.wait_ge(s_yc, b + 1)
                    for c in range(2):
                        mm = pe.transpose(bank(6 + slot)[0:P, 256 + c * 2 * T:256 + (c + 1) * 2 * T],
                                          y_tok[:, slot, c * P:(c + 1) * P], ident[0:2 * T, 0:2 * T])
                    mm.then_inc(s_yt, 1)

                def image(b, turn, slot, last=False):
                    first = isinstance(b, int) and b == 0
                    for c in range(STEPS):
                        wait_count(pe, s_sc, STEPS * b + c - 1)
                        spread(decay_ps(c), 0, c, slot, s_pdt)
                        d, cx = ahead(b, c)
                        if not (last and d):
                            spread_x(b + d, turn + (d if slot else 0), cx, slot ^ d)
                        if c == Y_STEP and not (isinstance(b, int) and b < 2):
                            turn_y(b - 2, slot)
                        if not first:
                            if c == 0:
                                pe.wait_ge(s_sc, STEPS * b)
                                pe.wait_ge(s_cb, 2 * b)
                            sums(1 - slot, share[c], share[c + 1])

                for c in range(LEAD):
                    spread_x(0, 0, c, 0)
                images(pe, image)
                pe.wait_ge(s_sc, STEPS * B)
                pe.wait_ge(s_cb, 2 * B)
                turn_y(B - 2, 0)
                sums((B - 1) % 2, 0, T)
                turn_y(B - 1, 1)

            @block.scalar
            def _(act):
                def copy_b(b, slot):
                    wait_count(act, s_u, PST * (b - 1))
                    wait_count(act, s_ud, b - 1)
                    act.copy(bb[:, slot, :], Bs[:, bass.ds(b * T, T)]).then_inc(s_bb, 1)

                def copy_c(b, slot):
                    wait_count(act, s_y, b - 1)
                    for u in range(2):
                        diag = c_diag[u * NS:(u + 1) * NS, slot, u * T:u * T + T * (2 * T + 1)]
                        act.copy(diag.rearrange("p (t x) -> p t x", x=2 * T + 1)[:, :, 0],
                                 Cs[u * NS:(u + 1) * NS, bass.ds(b * T, T)]).then_inc(s_cb, 1)

                def copy_y(b, slot):
                    act.wait_ge(s_y, b + 1)
                    act.copy(y_tok[:, slot, :], bank(6 + slot)[0:2 * T, 0:DI // 2]).then_inc(s_yc, 1)

                def copy_x(b, c):
                    if c >= PST:
                        return
                    act.wait_ge(s_px, STEPS * b + c + 1)
                    if c >= 4:
                        wait_count(act, s_u, PST * b + c - 3)
                    else:
                        wait_count(act, s_u, PST * (b - 1) + (c + 5 if c < 3 else c + 1))
                    act.copy(xs[:, c % 4, :], x_ps).then_inc(s_xs, 1)

                def image(b, turn, slot, last=False):
                    for c in range(STEPS):
                        act.wait_ge(s_pdt, STEPS * b + c + 1)
                        d = decay_ps(c).rearrange("p (f t) -> p f t", t=T)[:, :, 1:T]
                        act.activation(d, d, ACT.Exp, scale=a_neg[:, 0:1]).then_inc(s_da, 1)
                        if c == 0 and not (isinstance(b, int) and b < 2):
                            copy_y(b - 2, slot)
                        if c == 4:
                            copy_c(b, slot)
                            if not last:
                                copy_b(b + 1, 1 - slot)
                        dx, cx = ahead(b, c)
                        if not (last and dx):
                            copy_x(b + dx, cx)

                copy_b(0, 0)
                for c in range(LEAD):
                    copy_x(0, c)
                images(act, image)
                copy_y(B - 2, 0)
                copy_y(B - 1, 1)

            @block.gpsimd
            def _(pool):
                def image(b, turn, slot, last=False):
                    pool.wait_ge(s_bb, b + 1)
                    for c in range(PST):
                        pool.wait_ge(s_xs, PST * b + c + 1)
                        wait_count(pool, s_sc, STEPS * b + c - 3)
                        pool.tensor_tensor(u_[:, c % 4, :].rearrange("p (f t) -> p f t", t=T),
                                           xs[:, c % 4, :].rearrange("p (f t) -> p f t", t=T),
                                           bb[:, slot, :].unsqueeze(1).to_broadcast([128, GRP, T]),
                                           ALU.mult).then_inc(s_u, 1)

                images(pool, image)

            @block.vector
            def _(dve):
                def take_y(b, slot):
                    dve.wait_ge(s_yt, b + 1)
                    o = yT[:, :, bass.ds(b * T, T)].rearrange("p (u c) t -> p u c t", u=2)
                    dve.tensor_tensor(o, bank(6 + slot)[0:P, 256:256 + 4 * T].rearrange("p (c u t) -> p u c t", c=2, u=2),
                                      o, ALU.add)

                def image(b, turn, slot, last=False):
                    older = not (isinstance(b, int) and b < 2)
                    for c in range(STEPS):
                        if c == 0:
                            wait_count(dve, s_y, b - 1)
                        dve.wait_ge(s_da, STEPS * b + c + 1)
                        if c < PST:
                            dve.wait_ge(s_u, PST * b + c + 1)
                        else:
                            dve.wait_ge(s_ud, b + 1)
                        f = (c % (STEPS // 2)) * GRP
                        dve.tensor_tensor_scan(
                            hs[:, slot, c // (STEPS // 2), f:f + GRP, :].rearrange("p f t -> p (f t)"),
                            decay_ps(c), u_[:, c % 4, :], 0.0, ALU.mult, ALU.add).then_inc(s_sc, 1)
                        if c == Y_STEP + 2 and older:
                            take_y(b - 2, slot)
                        if c == PST - 2:
                            dve.wait_ge(s_px, STEPS * (b + 1))
                            dve.wait_ge(s_bb, b + 1)
                            dve.wait_ge(s_sc, STEPS * b + PST - 3)
                            dve.tensor_tensor(u_[:, PST % 4, :].rearrange("p (f t) -> p f t", t=T),
                                              x_ps.rearrange("p (f t) -> p f t", t=T),
                                              bb[:, slot, :].unsqueeze(1).to_broadcast([128, GRP, T]),
                                              ALU.mult).then_inc(s_ud, 1)

                images(dve, image)
                take_y(B - 2, 0)
                take_y(B - 1, 1)

        s_gy = sem("y_gated")
        s_po = sem("scan_out_done")
        with nc.Block() as block:
            @block.vector
            def _(dve):
                for m in range(KI):
                    dve.tensor_tensor(yT[:, m, :], yT[:, m, :], silu[:, m, :], ALU.mult).then_inc(s_gy, 1)
                for m in range(K):
                    dve.wait_ge(s_po, m + 1)
                    dve.tensor_tensor(h[:, m, :], h[:, m, :], bank(2 * m, 2)[0:P, 0:TOK], ALU.add)

            @block.tensor
            def _(pe):
                pe.wait_ge(s_wout, 16)
                pe.wait_ge(s_gy, KI)
                for m in range(K):
                    for a, b in WIDE:
                        for k in range(KI):
                            mm = pe.matmul(bank(2 * m, 2)[0:P, a:b], w_out[:, k, m * P:(m + 1) * P], yT[:, k, a:b],
                                           start=(k == 0), stop=(k == KI - 1))
                    mm.then_inc(s_po, 1)


def build_attention(nc, A, sem, sb_in, bank, g):
    h, ident, over, ones, eps, V = (g[n] for n in ("h", "ident", "over", "ones", "eps", "V"))
    xn, xc, sq, std = (g[n] for n in ("xn", "xc", "sq", "std"))
    STEPS = B // 2
    QPAD = TOK + 64 - T
    with ExitStack() as ctx:
        sb = sb_in(ctx)
        wq = sb("wq", [P, 2, K, NH, 32])
        wv = sb("wv", [P, K, D])
        wo = sb("wo", [128, NG, D])
        qk = sb("qk", [128, 2, NG, QPAD])
        v = sb("v_att", [T, B, NH, 32])
        pr = sb("pr_att", [128, 2, NH * T])
        mx = sb("mx", [128, 2, NH])
        pT = sb("pT", [T, 2, NH, 128])
        oT = sb("oT", [128, NG, TOK])
        y = sb("y_att", [P, K, TOK])

        s_z = sem("att_zeroed")
        s_w = sem("att_weights")
        s_qk = sem("qk_done")
        s_qke = sem("qk_copied")
        s_v = sem("v_done")
        s_ve = sem("v_copied")
        s_s = sem("scores_done")
        s_mx = sem("score_max")
        s_sub = sem("scores_shifted")
        s_exp = sem("scores_exp")
        s_sum = sem("prob_sum")
        s_rc = sem("prob_recip")
        s_pr = sem("probs_ready")
        s_pt = sem("probs_transposed")
        s_pe = sem("probs_copied")
        s_o = sem("heads_done")
        s_oe = sem("heads_copied")
        s_y = sem("att_out_done")
        s_ye = sem("att_out_copied")
        s_af = sem("att_affine")
        L = dict(g["norm"], base=LN_ATT)
        L2 = dict(g["norm"], base=LN_OUT)
        with nc.Block() as block:
            @block.sync
            def _(sp):
                sp.wait_ge(s_z, 2)
                wqkv = A["L1_attn_w_qkv"].rearrange("(k p) (w h d) -> p w k h d", p=P, w=3, h=NH)
                for w in range(2):
                    for k in range(K):
                        sp.dma_start(wq[:, w, k, :, 0:HD], wqkv[:, w, k, :, :]).then_inc(s_w, 16)
                sp.dma_start(wv[:, :, :], A["L1_attn_w_qkv"].rearrange("(k p) d -> p k d", p=P)[:, :, 2 * D:3 * D]).then_inc(s_w, 16)
                wo_v = A["L1_attn_w_out"].rearrange("(g j i) d -> j i g d", g=NG, j=HG)
                for j in range(HG):
                    sp.dma_start(wo[32 * j:32 * j + HD, :, :], wo_v[j]).then_inc(s_w, 16)

            @block.gpsimd
            def _(pool):
                pool.memset(wq[:, :, :, :, :], 0.0).then_inc(s_z, 1)
                pool.memset(wo[:, :, :], 0.0).then_inc(s_z, 1)
                pool.memset(qk[:, :, :, TOK:QPAD], 0.0).then_inc(s_z, 1)
                pool.memset(v[:, :, :, HD:32], 0.0).then_inc(s_z, 1)

            @block.tensor
            def _(pe):
                layer_norm_pe(pe, L, h, sq, over[:, :], [bank(0), bank(1)], [bank(2), bank(3)], HALVES)
                pe.wait_ge(L["out"], L["base"] + 2)
                pe.wait_ge(s_w, 9 * 16)
                pe.wait_ge(s_z, 4)
                for w in range(2):
                    for c in range(NG):
                        n = w * NG + c
                        if n >= 4:
                            pe.wait_ge(s_qke, n - 3)
                        for a, b in WIDE:
                            for k in range(K):
                                mm = pe.matmul(bank(2 * (n % 4), 2)[:, a:b],
                                               wq[:, w, k, HG * c:HG * c + HG, :].rearrange("p h d -> p (h d)"),
                                               xn[:, k, a:b], start=(k == 0), stop=(k == K - 1))
                        mm.then_inc(s_qk, 1)
                pe.wait_ge(s_qke, 2 * NG)
                for b in range(B):
                    if b >= 4:
                        pe.wait_ge(s_ve, b - 3)
                    for k in range(K):
                        mm = pe.matmul(bank(4 + b % 4)[0:T, 0:D], xn[:, k, b * T:(b + 1) * T], wv[:, k, :],
                                       start=(k == 0), stop=(k == K - 1))
                    mm.then_inc(s_v, 1)

                def scores(r):
                    if r >= 1:
                        pe.wait_ge(s_sub, r)
                    for c in range(NG):
                        for u in range(2):
                            t0 = (2 * r + u) * T
                            for j in range(HG):
                                mm = pe.matmul(bank(j)[64 * u:64 * u + 64, c * T:(c + 1) * T],
                                               qk[32 * j:32 * j + 32, 0, c, t0:t0 + 64],
                                               qk[32 * j:32 * j + 32, 1, c, t0:t0 + T], start=True, stop=True)
                    mm.then_inc(s_s, 1)

                def heads(r):
                    pe.wait_ge(s_pr, r + 1)
                    if r >= 1:
                        pe.wait_ge(s_pe, r)
                    for n in range(NH):
                        t = pe.transpose(bank(4 + n // 4)[0:T, (n % 4) * 128:(n % 4 + 1) * 128],
                                         pr[:, r % 2, n * T:(n + 1) * T], ident[:, :])
                    t.then_inc(s_pt, 1)

                def values(r):
                    pe.wait_ge(s_pe, r + 1)
                    if r >= 1:
                        pe.wait_ge(s_oe, r)
                    for c in range(NG):
                        for j in range(HG):
                            for u in range(2):
                                mm = pe.matmul(bank(7)[32 * j:32 * j + 32, (2 * c + u) * T:(2 * c + u + 1) * T],
                                               v[:, 2 * r + u, HG * c + j, :],
                                               pT[:, r % 2, j * NG + c, 64 * u:64 * u + T], start=True, stop=True)
                    mm.then_inc(s_o, 1)

                pe.wait_ge(s_ve, B)
                scores(0)
                for r in range(STEPS):
                    if r + 1 < STEPS:
                        scores(r + 1)
                    heads(r)
                    values(r)
                pe.wait_ge(s_oe, STEPS)
                for m in range(K):
                    for p, (a, b) in enumerate(HALVES):
                        for c in range(NG):
                            mm = pe.matmul(bank(4 + 2 * m + p)[0:P, 0:b - a], wo[:, c, m * P:(m + 1) * P], oT[:, c, a:b],
                                           start=(c == 0), stop=(c == NG - 1))
                        mm.then_inc(s_y, 1)
                pe.wait_ge(s_ye, 4)
                layer_norm_pe(pe, L2, y, sq, over[:, :], [bank(0), bank(1)], [bank(2), bank(3)], HALVES)

            @block.scalar
            def _(act):
                layer_norm_act(act, L, xc, sq, std, eps[0:P, :], [bank(2), bank(3)], HALVES)
                for n in range(2 * NG):
                    act.wait_ge(s_qk, n + 1)
                    act.copy(qk[:, n // NG, n % NG, 0:TOK], bank(2 * (n % 4), 2)[:, 0:TOK]).then_inc(s_qke, 1)
                for r in range(STEPS):
                    act.wait_ge(s_sub, r + 1)
                    act.activation(pr[:, r % 2, :], pr[:, r % 2, :], ACT.Exp, scale=HD ** -0.5).then_inc(s_exp, 1)
                    act.wait_ge(s_pt, r + 1)
                    if r >= 2:
                        act.wait_ge(s_o, r - 1)
                    act.copy(pT[:, r % 2, :, :].rearrange("p n q -> p (n q)"), bank(4, 3)[0:T, :]).then_inc(s_pe, 1)
                    act.wait_ge(s_o, r + 1)
                    act.copy(oT[:, :, 2 * r * T:2 * (r + 1) * T],
                             bank(7)[:, 0:2 * NG * T].rearrange("p (c q) -> p c q", c=NG)).then_inc(s_oe, 1)
                for m in range(K):
                    for p, (a, b) in enumerate(HALVES):
                        act.wait_ge(s_y, 2 * m + p + 1)
                        act.activation(y[:, m, a:b], bank(4 + 2 * m + p)[0:P, 0:b - a], ACT.Identity,
                                       bias=V[:, ROW_BOUT + m:ROW_BOUT + m + 1]).then_inc(s_ye, 1)
                layer_norm_act(act, L2, xc, sq, std, eps[0:P, :], [bank(2), bank(3)], HALVES)
                act.wait_ge(L2["out"], L2["base"] + 2)
                for k in range(K):
                    act.activation(y[:, k, :], y[:, k, :], ACT.Identity, bias=V[:, ROW_LNB + k:ROW_LNB + k + 1],
                                   scale=V[:, ROW_LNG + k:ROW_LNG + k + 1]).then_inc(s_af, 1)

            @block.vector
            def _(dve):
                layer_norm_dve(dve, L, h, xc, std, xn, [bank(0), bank(1)], HALVES)
                for b in range(B):
                    dve.wait_ge(s_v, b + 1)
                    dve.tensor_copy(v[:, b, :, 0:HD], bank(4 + b % 4)[0:T, 0:D].rearrange("p (h d) -> p h d", d=HD)).then_inc(s_ve, 1)
                for r in range(STEPS):
                    s = r % 2
                    sv = bank(0, 4).rearrange("p (j f) -> p j f", j=HG)[:, :, 0:NG * T].rearrange("p j (c t) -> p j c t", c=NG)
                    pv = pr[:, s, :].rearrange("p (j c t) -> p j c t", j=HG, c=NG)
                    pn = pr[:, s, :].rearrange("p (n t) -> p n t", n=NH)
                    mv = mx[:, s, :].rearrange("p (j c) -> p j c", j=HG)
                    dve.wait_ge(s_s, r + 1)
                    dve.tensor_reduce(mv, sv, AX_X, ALU.max).then_inc(s_mx, 1)
                    dve.wait_ge(s_mx, r + 1)
                    if r >= 2:
                        dve.wait_ge(s_pt, r - 1)
                    dve.tensor_tensor(pv, sv, mv.unsqueeze(3).to_broadcast([128, HG, NG, T]), ALU.subtract).then_inc(s_sub, 1)
                    dve.wait_ge(s_exp, r + 1)
                    dve.tensor_reduce(mx[:, s, :], pn, AX_X, ALU.add).then_inc(s_sum, 1)
                    dve.wait_ge(s_sum, r + 1)
                    dve.reciprocal(mx[:, s, :], mx[:, s, :]).then_inc(s_rc, 1)
                    dve.wait_ge(s_rc, r + 1)
                    dve.tensor_tensor(pn, pn, mx[:, s, :].unsqueeze(2).to_broadcast([128, NH, T]), ALU.mult).then_inc(s_pr, 1)
                layer_norm_dve(dve, L2, y, xc, std, y, [bank(0), bank(1)], HALVES)
                for k in range(K):
                    dve.wait_ge(s_af, k + 1)
                    dve.tensor_tensor(h[:, k, :], h[:, k, :], y[:, k, :], ALU.add)


def build_moe(nc, A, sem, sb_in, bank, g, layer, out=None):
    h, ident, over, ones, eps, V, VB = (g[n] for n in ("h", "ident", "over", "ones", "eps", "V", "VB"))
    xn, xc, sq, std = (g[n] for n in ("xn", "xc", "sq", "std"))
    tag = f"moe{layer}"
    H = (H0, H1)[layer]
    MC = H // 128
    row_b1 = (ROW_B0, ROW_B1)[layer]
    gelu = (ACT.Gelu_apprx_tanh, ACT.Gelu)[layer]
    W1, W2, b2_d = ((A["L0_ffn_w1"], A["L0_ffn_w2"], A["L0_ffn_b2"]),
                    (A["L1_ffn_W1"], A["L1_ffn_W2"], A["L1_ffn_b2"]))[layer]
    CAP = 2 * TOK
    LAST = TOK - 4 * 128
    NB2 = 3
    with ExitStack() as ctx:
        sb = sb_in(ctx, f"{tag}_")
        w1 = [sb(f"w1_{s}", [P, K, H]) for s in range(2)]
        w2 = [sb(f"w2_{s}", [128, MC, D]) for s in range(2)]
        hid = [sb(f"hid_{s}", [128, MC, TPAD]) for s in range(2)]
        acc = sb("acc", [128, TT5, D])
        b2 = sb("b2", [E, D])
        gate = sb("gate", [128, TT5, E])
        gT = sb("gT", [E, TPAD])
        sc = sb("sc", [128, TT5, E])
        ex = sb("ex", [128, TT5, E])
        m1 = sb("m1", [128, TT5])
        valid = sb("valid", [128, 2])

        s_w1 = [sem(f"{tag}_w1_{s}") for s in range(2)]
        s_w2 = [sem(f"{tag}_w2_{s}") for s in range(2)]
        s_b2 = sem(f"{tag}_b2")
        s_pad = sem(f"{tag}_padded")
        s_m1 = sem(f"{tag}_first_product")
        s_hid = sem(f"{tag}_hidden")
        s_m2 = sem(f"{tag}_second_product")
        s_acc = sem(f"{tag}_accumulated")
        s_fin = sem(f"{tag}_sum_transposed")
        s_lg = sem(f"{tag}_logits")
        s_ch = sem(f"{tag}_chain")
        s_ei = sem(f"{tag}_exp_in")
        s_ex = sem(f"{tag}_exp")
        s_ct = sem(f"{tag}_counted")
        s_tt = sem(f"{tag}_total")
        s_sT = sem(f"{tag}_scores_ready")
        s_sTp = sem(f"{tag}_scores_transposed")
        s_oi = sem(f"{tag}_offset_in")
        s_of = sem(f"{tag}_offset")
        s_g = sem(f"{tag}_gates")
        s_gp = sem(f"{tag}_gates_transposed")
        s_gd = sem(f"{tag}_gates_copied")
        s_o = sem(f"{tag}_stored")
        L = dict(g["norm"], base=(LN_MOE0, LN_MOE1)[layer])
        w_g = tri = scT = eq = pre = cnt = T_ = cand = bitv = lim = keys = oh = None
        if layer == 0:
            tri = sb("tri", [E, E])
            scT = sb("scT", [E, TPAD])
            eq = sb("eq", [E, TOK])
            pre = sb("pre", [E, TOK])
            ones_r = sb("ones_r", [E, TOK])
            cnt = sb("cnt", [128, 1])
            T_ = sb("thr", [128, 1], I32)
            cand = sb("cand", [128, 1], I32)
            bitv = sb("bitv", [128, 1], I32)
            need = sb("need", [128, 1])
            lim = sb("lim", [E, 1])
        else:
            w_g = sb("w_g", [P, K, E])
            s_wg = sem("w_g_loaded")
            em = sb("em", [128, TT5, E])
            key = sb("key", [128, TT5, E])
            oh = [sb(f"oh_{n}", [128, TT5, E]) for n in range(2)]
            top = [sb(f"top_{n}", [128, TT5]) for n in range(2)]
            pr = [sb(f"pr_{n}", [128, TT5]) for n in range(2)]
            fin = sb("fin", [128, TT5, D])

        BITS = list(range(29, -1, -1))

        with nc.Block() as block:
            @block.sync
            def _(sp):
                def load1(e, s):
                    sp.dma_start(w1[s][:, :, :], W1[bass.ds(e, 1)].rearrange("a (k p) d -> p (a k) d", p=P)).then_inc(s_w1[s], 16)

                def load2(e, s):
                    sp.dma_start(w2[s][:, :, :], W2[bass.ds(e, 1)].rearrange("a (m p) d -> p (a m) d", p=128)).then_inc(s_w2[s], 16)

                if layer == 1:
                    sp.dma_start(w_g[:, :, :], A["L1_ffn_Wg"].rearrange("(k p) e -> p k e", p=P)).then_inc(s_wg, 16)
                sp.dma_start(b2[:, :], b2_d).then_inc(s_b2, 16)
                for s in range(2):
                    load1(s, s)
                    load2(s, s)
                for s in range(2):
                    sp.wait_ge(s_m1, MC * (s + 1))
                    load1(s + 2, s)
                with sp.Fori(1, E // 2 - 1) as i:
                    for s in range(2):
                        sp.wait_ge(s_m2, NB2 * (2 * i + s - 1))
                        load2(2 * i + s, s)
                        sp.wait_ge(s_m1, MC * (2 * i + s + 1))
                        load1(2 * i + s + 2, s)
                for e in range(E - 2, E):
                    sp.wait_ge(s_m2, NB2 * (e - 1))
                    load2(e, e % 2)
                if layer == 1:
                    ov = out.rearrange("b t d -> (b t) d")
                    sp.wait_ge(s_fin, TT5 + TT5)
                    sp.dma_start(ov[0:512].rearrange("(i p) d -> p i d", p=128), fin[:, 0:4, :]).then_inc(s_o, 16)
                    sp.dma_start(ov[512:TOK], fin[0:LAST, 4, :]).then_inc(s_o, 16)
                    sp.wait_ge(s_o, 32)

            @block.gpsimd
            def _(pool):
                pool.memset(xn[:, :, TOK:TPAD], 0.0).then_inc(s_pad, 1)
                pool.memset(valid[:, 0:1], 1.0).then_inc(s_pad, 1)
                pool.memset(valid[:, 1:2], 0.0).then_inc(s_pad, 1)
                for s in range(2):
                    pool.memset(hid[s][:, :, TOK:TPAD], 0.0).then_inc(s_pad, 1)
                pool.wait_ge(s_pad, 5)
                for c, fill in ((0, 0.0), (1, -1.0)):
                    pool.affine_select(out=valid[:, c:c + 1], in_=valid[:, c:c + 1], compare_op=ALU.is_ge, fill=fill,
                                       base=LAST - 1, pattern=[[0, 1]], channel_multiplier=-1).then_inc(s_pad, 1)
                if layer == 0:
                    pool.memset(T_[:, :], 0).then_inc(s_pad, 1)
                    pool.memset(cand[:, :], 1 << BITS[0]).then_inc(s_pad, 1)
                    pool.memset(scT[:, :], 0.0).then_inc(s_pad, 1)
                    pool.memset(ones_r[:, :], 1.0).then_inc(s_pad, 1)
                    pool.memset(gT[:, :], 0.0).then_inc(s_pad, 1)
                    pool.affine_select(out=tri[:, :], in_=ones[0:E, 0:E], compare_op=ALU.is_ge, fill=0.0,
                                       base=-1, pattern=[[1, E]], channel_multiplier=-1).then_inc(s_pad, 1)
                else:
                    for e in range(E):
                        pool.memset(em[:, :, e:e + 1], float(e - E)).then_inc(s_pad, 1)

            n_pad = 13 if layer == 0 else 7 + E

            @block.tensor
            def _(pe):
                layer_norm_pe(pe, L, h, sq, over[:, :], [bank(0), bank(1)], [bank(2), bank(3)], HALVES)
                pe.wait_ge(L["out"], L["base"] + 2)
                pe.wait_ge(s_pad, n_pad)
                if layer == 1:
                    pe.wait_ge(s_wg, 16)
                wg = w_g if layer == 1 else V[:, ROW_GW:ROW_GW + K * E].rearrange("p (e k) -> p k e", k=K)
                for i in range(TT5):
                    for k in range(K):
                        mm = pe.matmul(bank(7)[:, i * E:(i + 1) * E], xn[:, k, i * 128:(i + 1) * 128], wg[:, k, :],
                                       start=(k == 0), stop=(k == K - 1))
                mm.then_inc(s_lg, 1)

                def total(n):
                    pe.wait_ge(s_ct, n + 1)
                    pe.matmul(bank(7)[:, 64:65], ones[:, :], cnt[:, :], start=True, stop=True).then_inc(s_tt, 1)

                def product1(e, s, turn, opening=False, between=None):
                    pe.wait_ge(s_w1[s], 16 * (turn + 1))
                    for m in range(MC):
                        if not (opening and e == 0 and m < 2):
                            pe.wait_ge(s_hid, MC * e + m - 1)
                        for a, b in WIDE:
                            for k in range(K):
                                mm = pe.matmul(bank(2 * ((s * MC + m) % 2), 2)[:, a:b], w1[s][:, k, m * 128:(m + 1) * 128],
                                               xn[:, k, a:b], start=(k == 0), stop=(k == K - 1))
                            if b == TOK:
                                mm.then_inc(s_m1, 1)
                            if between:
                                between()

                def product2(e, s, turn, opening=False):
                    pe.wait_ge(s_w2[s], 16 * (turn + 1))
                    pe.wait_ge(s_hid, MC * (e + 1))
                    for j in range(NB2):
                        if not opening:
                            pe.wait_ge(s_acc, NB2 * e - NB2 + j + 1)
                        for i in range(2 * j, min(2 * j + 2, TT5)):
                            for m in range(MC):
                                mm = pe.matmul(bank(4 + j)[:, (i % 2) * D:(i % 2 + 1) * D],
                                               hid[s][:, m, i * 128:(i + 1) * 128], w2[s][:, m, :],
                                               start=(m == 0), stop=(m == MC - 1))
                        mm.then_inc(s_m2, 1)

                rounds = list(range(len(BITS) + 1)) if layer == 0 else []

                def one_round():
                    if rounds:
                        total(rounds.pop(0))

                product1(0, 0, 0, opening=True, between=one_round)
                product1(1, 1, 0, between=one_round)
                while rounds:
                    one_round()
                if layer == 0:
                    pe.wait_ge(s_sT, 1)
                    for i in range(TT5):
                        t = pe.transpose(bank(5, 2)[0:E, i * 128:(i + 1) * 128], sc[:, i, :], ident[:, :])
                    t.then_inc(s_sTp, 1)
                    pe.wait_ge(s_oi, 1)
                    pe.matmul(bank(7)[0:E, 66:67], tri[:, :], pre[:, TOK - 1:TOK], start=True, stop=True).then_inc(s_of, 1)
                    pe.wait_ge(s_g, 1)
                    for i in range(TT5):
                        t = pe.transpose(bank(7)[:, 128 + i * E:128 + (i + 1) * E], gT[:, i * 128:(i + 1) * 128], ident[0:E, 0:E])
                    t.then_inc(s_gp, 1)
                else:
                    pe.wait_ge(s_gd, 1)
                    for i in range(TT5):
                        t = pe.transpose(bank(5, 2)[0:E, i * 128:(i + 1) * 128], gate[:, i, :], ident[:, :])
                    t.then_inc(s_gp, 1)
                    pe.wait_ge(s_g, 1)
                product2(0, 0, 0, opening=True)
                product1(2, 0, 1)
                product2(1, 1, 0)
                product1(3, 1, 1)
                with pe.Fori(1, E // 2 - 1) as i:
                    for s in range(2):
                        product2(2 * i + s, s, i)
                        product1(2 * i + s + 2, s, i + 1)
                product2(E - 2, 0, E // 2 - 1)
                product2(E - 1, 1, E // 2 - 1)
                pe.wait_ge(s_acc, NB2 * E)
                pe.wait_ge(s_b2, 16)
                if layer == 0:
                    for m in range(K):
                        for i in range(TT5):
                            n = 128 if i < TT5 - 1 else LAST
                            o = bank(2 * m, 2)[0:P, i * 128:i * 128 + n]
                            pe.matmul(o, b2[:, m * P:(m + 1) * P], gT[:, i * 128:i * 128 + n], start=True, stop=False)
                            mm = pe.matmul(o, acc[:, i, m * P:(m + 1) * P], ident[:, 0:n], start=False, stop=True)
                        mm.then_inc(s_fin, 1)
                else:
                    for i in range(TT5):
                        n = 128 if i < TT5 - 1 else LAST
                        pe.matmul(bank(i)[0:n, 0:D], gT[:, i * 128:i * 128 + n], b2[:, :], start=True, stop=False,
                                  skip_group_check=True)
                        for k in range(K):
                            mm = pe.matmul(bank(i)[0:n, k * P:(k + 1) * P], h[:, k, i * 128:i * 128 + n],
                                           ident[0:P, 0:P], start=False, stop=(k == K - 1), skip_group_check=True)
                        mm.then_inc(s_fin, 1)

            @block.scalar
            def _(act):
                layer_norm_act(act, L, xc, sq, std, eps[0:P, :], [bank(2), bank(3)], HALVES)
                act.wait_ge(s_ei, 1)
                if layer == 0:
                    act.activation(ex[:, :, :], sc[:, :, :], ACT.Exp).then_inc(s_ex, 1)
                else:
                    act.activation(pr[1][:, :], m1[:, :], ACT.Exp).then_inc(s_ex, 1)
                act.wait_ge(s_pad, n_pad)

                def expert(e, s, opening=False):
                    for m in range(MC):
                        act.wait_ge(s_m1, MC * e + m + 1)
                        if m == 0 and not opening:
                            act.wait_ge(s_m2, NB2 * (e - 1))
                        act.activation(hid[s][:, m, 0:TOK], bank(2 * ((s * MC + m) % 2), 2)[:, 0:TOK], gelu,
                                       bias=VB[:, bass.ds(row_b1 + MC * e + m, 1)]).then_inc(s_hid, 1)

                expert(0, 0, opening=True)
                expert(1, 1, opening=True)
                with act.Fori(1, E // 2) as i:
                    for s in range(2):
                        expert(2 * i + s, s)

            @block.vector
            def _(dve):
                layer_norm_dve(dve, L, h, xc, std, xn, [bank(0), bank(1)], HALVES)
                chain = [0]

                def link(ins):
                    chain[0] += 1
                    ins.then_inc(s_ch, 1)
                    dve.wait_ge(s_ch, chain[0])

                def over_e(x):
                    return x.unsqueeze(2).to_broadcast([128, TT5, E])

                dve.wait_ge(s_lg, 1)
                dve.wait_ge(s_pad, n_pad)
                lg = bank(7)[:, 0:TT5 * E].rearrange("p (i e) -> p i e", e=E)
                if layer == 0:
                    link(dve.tensor_reduce(m1[:, :], lg, AX_X, ALU.max))
                    dve.tensor_tensor(sc[:, :, :], lg, over_e(m1[:, :]), ALU.subtract).then_inc(s_ei, 1)
                    dve.wait_ge(s_ex, 1)
                    link(dve.tensor_reduce(m1[:, :], ex[:, :, :], AX_X, ALU.add))
                    link(dve.reciprocal(m1[:, :], m1[:, :]))
                    link(dve.tensor_tensor(sc[:, :, :], ex[:, :, :], over_e(m1[:, :]), ALU.mult))
                    link(dve.tensor_scalar(sc[:, TT5 - 1, :], sc[:, TT5 - 1, :], valid[:, 0:1], valid[:, 1:2],
                                           ALU.mult, ALU.add))
                    for n, bit in enumerate(BITS):
                        dve.tensor_scalar(ex[:, :, :], sc[:, :, :], cand[:, :].bitcast(F32), None, ALU.is_ge, ALU.add,
                                          accum_out=cnt[:, :]).then_inc(s_ct, 1)
                        dve.wait_ge(s_tt, n + 1)
                        link(dve.tensor_scalar(bitv[:, :], bank(7)[:, 64:65], float(CAP), float(1 << bit), ALU.is_ge, ALU.mult))
                        link(dve.tensor_tensor(T_[:, :], T_[:, :], bitv[:, :], ALU.bitwise_or))
                        if bit:
                            link(dve.tensor_scalar(cand[:, :], T_[:, :], 1 << (bit - 1), None, ALU.bitwise_or))
                    thr = T_[:, :].bitcast(F32)
                    dve.tensor_scalar(ex[:, :, :], sc[:, :, :], thr, None, ALU.is_gt, ALU.add,
                                      accum_out=cnt[:, :]).then_inc(s_ct, 1)
                    dve.wait_ge(s_tt, len(BITS) + 1)
                    dve.tensor_scalar(need[:, :], bank(7)[:, 64:65], -1.0, float(CAP), ALU.mult, ALU.add).then_inc(s_sT, 1)
                    dve.wait_ge(s_sTp, 1)
                    link(dve.tensor_copy(scT[:, 0:TOK], bank(5, 2)[0:E, 0:TOK]))
                    link(dve.tensor_scalar(eq[:, :], scT[:, 0:TOK], thr[0:E, :], None, ALU.is_equal))
                    dve.tensor_tensor_scan(pre[:, :], ones_r[:, :], eq[:, :], 0.0, ALU.mult, ALU.add).then_inc(s_oi, 1)
                    dve.wait_ge(s_of, 1)
                    link(dve.tensor_tensor(lim[:, :], need[0:E, :], bank(7)[0:E, 66:67], ALU.subtract))
                    link(dve.scalar_tensor_tensor(eq[:, :], pre[:, :], lim[:, 0:1], eq[:, :], ALU.is_le, ALU.mult))
                    link(dve.scalar_tensor_tensor(pre[:, :], scT[:, 0:TOK], thr[0:E, :], eq[:, :], ALU.is_gt, ALU.add))
                    dve.tensor_tensor(gT[:, 0:TOK], pre[:, :], scT[:, 0:TOK], ALU.mult).then_inc(s_g, 1)
                    dve.wait_ge(s_gp, 1)
                    link(dve.tensor_copy(gate[:, :, :].rearrange("p i e -> p (i e)"), bank(7)[:, 128:128 + TT5 * E]))
                else:
                    link(dve.tensor_copy(sc[:, :, :], lg))
                    for n in range(2):
                        link(dve.tensor_reduce(top[n][:, :], sc[:, :, :], AX_X, ALU.max))
                        link(dve.tensor_tensor(key[:, :, :], sc[:, :, :], over_e(top[n][:, :]), ALU.is_equal))
                        link(dve.tensor_tensor(key[:, :, :], key[:, :, :], em[:, :, :], ALU.mult))
                        link(dve.tensor_reduce(m1[:, :], key[:, :, :], AX_X, ALU.min))
                        link(dve.tensor_tensor(oh[n][:, :, :], key[:, :, :], over_e(m1[:, :]), ALU.is_equal))
                        if n == 0:
                            link(dve.scalar_tensor_tensor(sc[:, :, :], oh[0][:, :, :], -3e38, sc[:, :, :], ALU.mult, ALU.add))
                    dve.tensor_tensor(m1[:, :], top[1][:, :], top[0][:, :], ALU.subtract).then_inc(s_ei, 1)
                    dve.wait_ge(s_ex, 1)
                    link(dve.tensor_scalar(pr[0][:, :], pr[1][:, :], 1.0, None, ALU.add))
                    link(dve.reciprocal(pr[0][:, :], pr[0][:, :]))
                    link(dve.tensor_tensor(pr[1][:, :], pr[1][:, :], pr[0][:, :], ALU.mult))
                    for n in range(2):
                        link(dve.tensor_tensor(oh[n][:, :, :], oh[n][:, :, :], over_e(pr[n][:, :]), ALU.mult))
                    dve.tensor_tensor(gate[:, :, :], oh[0][:, :, :], oh[1][:, :, :], ALU.add).then_inc(s_gd, 1)
                    dve.wait_ge(s_gp, 1)
                    dve.tensor_copy(gT[:, :], bank(5, 2)[0:E, 0:TPAD]).then_inc(s_g, 1)

                def accumulate(e, opening=False):
                    for j in range(NB2):
                        dve.wait_ge(s_m2, NB2 * e + j + 1)
                        if not opening:
                            dve.wait_ge(s_acc, NB2 * e + j - NB2 + 1)
                        for i in range(2 * j, min(2 * j + 2, TT5)):
                            o = bank(4 + j)[:, (i % 2) * D:(i % 2 + 1) * D]
                            gs = gate[:, i, bass.ds(e, 1)]
                            if opening:
                                a = dve.tensor_scalar(acc[:, i, :], o, gs, None, ALU.mult)
                            else:
                                a = dve.scalar_tensor_tensor(acc[:, i, :], o, gs, acc[:, i, :], ALU.mult, ALU.add)
                        a.then_inc(s_acc, 1)

                accumulate(0, opening=True)
                accumulate(1)
                with dve.Fori(1, E // 2) as i:
                    for s in range(2):
                        accumulate(2 * i + s)
                if layer == 0:
                    for m in range(K):
                        dve.wait_ge(s_fin, m + 1)
                        dve.tensor_tensor(h[:, m, :], h[:, m, :], bank(2 * m, 2)[0:P, 0:TOK], ALU.add)
                else:
                    for i in range(TT5):
                        n = 128 if i < TT5 - 1 else LAST
                        dve.wait_ge(s_fin, TT5)
                        dve.tensor_tensor(fin[0:n, i, :], acc[0:n, i, :], bank(i)[0:n, 0:D], ALU.add).then_inc(s_fin, 1)


_INS = [
    'x', 'L0_tok_ln1_g', 'L0_tok_ln1_b', 'L0_tok_W_lin', 'L0_tok_b_lin', 'L0_tok_ln2_g', 'L0_tok_ln2_b',
    'L0_tok_pos_embedding', 'L0_tok_cls_token', 'L0_attn_W_in', 'L0_attn_W_x', 'L0_attn_W_dt', 'L0_attn_b_dt',
    'L0_attn_A_log', 'L0_attn_D', 'L0_attn_W_out', 'L0_ffn_gate_weight', 'L0_ffn_w1', 'L0_ffn_b1', 'L0_ffn_w2',
    'L0_ffn_b2', 'L1_attn_w_qkv', 'L1_attn_w_out', 'L1_attn_b_out', 'L1_attn_ln_g', 'L1_attn_ln_b', 'L1_ffn_Wg',
    'L1_ffn_W1', 'L1_ffn_b1', 'L1_ffn_W2', 'L1_ffn_b2']


def kernel(**inputs):
    import numpy as _np
    import concourse.bacc as _bacc
    from concourse.bass_utils import run_bass_kernel_spmd as _run

    nc = _bacc.Bacc("TRN2", target_bir_lowering=False, num_devices=1)
    arrays, aps = {}, {}
    for name in _INS:
        a = _np.ascontiguousarray(inputs[name])
        arrays[f"in_{name}"] = a
        aps[name] = nc.dram_tensor(f"in_{name}", a.shape, mybir.dt.from_np(a.dtype), kind="ExternalInput").ap()
    shape = (B, T, D)
    out = nc.dram_tensor("out_tokens", shape, F32, kind="ExternalOutput").ap()
    build_tower(nc, aps, out)
    r = _run(nc, [arrays], core_ids=[0])
    return r.results[0]["out_tokens"]
```
